# Optimizing a Trainium2 kernel written in Bass

```python
import numpy as np
import jax
import jax.numpy as jnp

def _softmax(x, axis=-1):
    return jax.nn.softmax(x, axis=axis)
def _gelu(x):
    return jax.nn.gelu(x, approximate=True)
def _silu(x):
    return jax.nn.silu(x)
def _sigmoid(x):
    return jax.nn.sigmoid(x)
def _layernorm(x, axis=-1, eps=1e-5):
    m = jnp.mean(x, axis=axis, keepdims=True)
    v = jnp.var(x, axis=axis, keepdims=True)
    return (x - m) / jnp.sqrt(v + eps)
def _scatter_add(tgt, idx, src, axis=0):
    return tgt.at[idx].add(src)
def _segment_sum(src, seg, n):
    return jax.ops.segment_sum(src, seg, n)

kernel_name = 'mk_adj_resnorm_d1_adj_256_bc86ed'

def setup_inputs(seed: int = 0):
    np.random.seed(seed)
    _w = jnp.asarray
    def _rec_inputs():
        import jax
        import jax.numpy as jnp
        _gk = jax.random.key(seed)
        x = -0.0005146 + 1 * jax.random.normal(jax.random.fold_in(_gk, 1), (8, 2048, 256), jnp.float32)
        _a = jax.random.bernoulli(jax.random.fold_in(_gk, 2), 0.00390625, (8, 2048, 2048))
        _a = jnp.logical_or(_a, jnp.swapaxes(_a, -1, -2))
        _a = jnp.logical_or(_a, jnp.eye(2048, dtype=bool))
        adj = _a.astype(jnp.int32)
        return x, adj
    x, adj = _rec_inputs()
    def _L0_gnn_setup():
        import jax, jax.numpy as jnp
        import numpy as np
        B, N, C, OUT, S = (4, 2048, 256, 256, 25)
        DENSITY = 0.008
        key = jax.random.key(seed)
        kA, kX, kW = jax.random.split(key, 3)
        A = jax.random.bernoulli(kA, DENSITY, (B, N, N)).astype(jnp.int32)
        X = jax.random.normal(kX, (B, N, C), dtype=jnp.float32)
        W = jax.random.normal(kW, (2 * C, OUT), dtype=jnp.float32) * np.float32(1.0 / np.sqrt(2 * C))
        b = jnp.zeros((OUT,), dtype=jnp.float32)
        return {'A': A, 'X': X, 'W': W, 'b': b}
    _L0_gnn_all = _L0_gnn_setup()
    _L0_gnn_in = {k: v for k, v in _L0_gnn_all.items() if k in ('W', 'b', )}
    del _L0_gnn_all

    return {
        "x": x,
        "adj": adj,
        "L0_gnn_W": _L0_gnn_in["W"],
        "L0_gnn_b": _L0_gnn_in["b"],
    }

def reference(x, adj, L0_gnn_W, L0_gnn_b):
    import jax
    import jax.numpy as jnp
    def _L0_gnn_ref(A, X, W, b):
        import jax, jax.numpy as jnp
        import numpy as np
        B, N, C, OUT, S = (4, 2048, 256, 256, 25)
        DENSITY = 0.008
        mask = A != 0
        neg_inf = jnp.float32(-jnp.inf)
        pri = -jnp.arange(N, dtype=jnp.float32)
        scores = jnp.where(mask, pri, neg_inf)
        vals, idx = jax.lax.top_k(scores, S)
        valid = vals > neg_inf
        feats = jax.vmap(lambda x, i: x[i])(X, idx)
        feats = jnp.where(valid[..., None], feats, neg_inf)
        agg = feats.max(axis=2)
        degree = mask.sum(axis=-1)
        agg = jnp.where((degree <= S)[..., None], jnp.maximum(agg, 0.0), agg)
        h = jnp.concatenate([X, agg], axis=-1)
        out = jax.nn.relu(jnp.einsum('bnf,fo->bno', h, W) + b)
        return out

    x = _layernorm(x + _L0_gnn_ref(adj, x, L0_gnn_W, L0_gnn_b), axis=-1)
    return x


_drawn_inputs = setup_inputs


def setup_inputs(seed=0):
    import zlib

    import numpy as np

    out = dict(_drawn_inputs(seed))
    spreads = {'L0_gnn_b': (0.0, 0.1)}
    factors = {}
    for name, (base, spread) in spreads.items():
        noise = np.random.default_rng([zlib.crc32(name.encode()), seed]).standard_normal(out[name].shape)
        drawn = base * np.exp(spread * noise) if base else spread * noise
        out[name] = jnp.asarray(drawn.astype(out[name].dtype))
    for name, factor in factors.items():
        out[name] = (out[name] * factor).astype(out[name].dtype)
    return out
```

```python
from contextlib import ExitStack

import concourse.bass as bass
from concourse import mybir
from concourse.alu_op_type import AluOpType as ALU

P = 128
S = 25
TOP = 32
U = 4
EPS = 1e-5
BIG = 3.0e38

ACT = mybir.ActivationFunctionType
F32 = mybir.dt.float32
I32 = mybir.dt.int32
AX_X = mybir.AxisListType.X


def build(nc: bass.Bass, x: bass.AP, adj: bass.AP, w: bass.AP, bias: bass.AP, out: bass.AP):
    B, N, C = x.shape
    OUT = w.shape[1]
    NT = B * N // P
    TPB = N // P
    KC = C // P
    LAST = NT + 2

    x_rows = x.rearrange("b n c -> (b n) c")
    adj_rows = adj.rearrange("b n m -> (b n) m")
    out_rows = out.rearrange("b n c -> (b n) c")

    with ExitStack() as ctx:
        def sb(name, shape, dt=F32):
            return ctx.enter_context(nc.sbuf_tensor(name, shape, dt))

        def pb(name, shape, dt=F32):
            return ctx.enter_context(nc.psum_tensor(name, shape, dt))

        def sem(name):
            return ctx.enter_context(nc.semaphore(name))

        adj_sb = sb("adj_sb", [P, 2, N], I32)
        x_sb = sb("x_sb", [P, U, C])
        score = sb("score", [P, N])
        place = sb("place", [P, N])
        idx_base = sb("idx_base", [P, NT])
        top = sb("top", [P, 2, TOP])
        filled = sb("filled", [P, TOP])
        idx = sb("idx", [P, 2, TOP], I32)
        floor = sb("floor", [P, 2, 2])
        gath = sb("gath", [P, 2, S, C])
        agg = sb("agg", [P, 2, C])
        hT = sb("hT", [P, 2, 2 * KC, P])
        w_sb = sb("w_sb", [P, 2 * KC, OUT])
        bias_sb = sb("bias_sb", [1, OUT])
        ones = sb("ones", [1, P])
        ident = sb("ident", [P, P])
        z = sb("z", [P, 2, OUT])
        stats = sb("stats", [P, 6])
        mv = sb("mv", [P, 2, 2])
        eps_sb = sb("eps_sb", [P, 1])
        std = sb("std", [P, 2])
        scale = sb("scale", [P, 2, 2])
        res = sb("res", [P, 2, OUT])

        ps_t = [pb(f"ps_t{i}", [P, 2 * KC, P]) for i in range(2)]
        ps_y = [pb(f"ps_y{i}", [P, OUT]) for i in range(2)]

        adj_in = [sem(f"adj_in{i}") for i in range(2)]
        x_in = [sem(f"x_in{i}") for i in range(U)]
        w_in = sem("w_in")
        out_done = [sem(f"out_done{i}") for i in range(2)]
        gath_in = [sem(f"gath_in{i}") for i in range(2)]
        const_z = sem("const_z")
        const_p = sem("const_p")
        adj_free = sem("adj_free")
        x_free = sem("x_free")
        idx_ready = sem("idx_ready")
        gath_free = sem("gath_free")
        gath_begun = sem("gath_begun")
        agg_ready = sem("agg_ready")
        hT_psum = sem("hT_psum")
        hT_ready = sem("hT_ready")
        y_ready = sem("y_ready")
        var_ready = sem("var_ready")
        std_ready = sem("std_ready")
        scale_ready = sem("scale_ready")
        res_ready = sem("res_ready")
        dve_step = sem("dve_step")

        block = ctx.enter_context(nc.Block())

        def steps(eng, step, last):
            for u in range(U):
                step(0, u)
            with eng.Fori(1, NT // U) as i:
                for u in range(U):
                    step(i, u)
            for s in range(NT, last):
                step(NT // U, s - NT)

        def lagged(i, u, lag):
            if isinstance(i, int):
                t = U * i + u - lag
                return divmod(t, U) if 0 <= t < NT else None
            return (i, u - lag) if u >= lag else (i - 1, u - lag + U)

        def tile(i, u):
            return U * i + u

        def use(i, u):
            return U // 2 * i + u // 2

        @block.sync
        def _(sp):
            sp.dma_start(w_sb[:], w.rearrange("(k p) o -> p k o", p=P)).then_inc(w_in, 16)
            sp.dma_start(bias_sb[:], bias.rearrange("(a o) -> a o", a=1)).then_inc(w_in, 16)

            def step(i, u):
                if lagged(i, u, 0) is None:
                    return
                t = tile(i, u)
                sp.wait_ge(adj_free, t + 1)
                sp.dma_start(adj_sb[:, u % 2, :], adj_rows[bass.ds(t * P, P), :]).then_inc(adj_in[u % 2], 16)
                sp.wait_ge(x_free, t + 1)
                sp.dma_start(x_sb[:, u, :], x_rows[bass.ds(t * P, P), :]).then_inc(x_in[u], 16)

            steps(sp, step, NT)

        @block.gpsimd
        def _(pool):
            pool.memset(ident[:], 0.0).then_inc(const_z, 1)
            pool.wait_ge(const_z, 1)
            pool.affine_select(out=ident[:], in_=ident[:], compare_op=ALU.not_equal, fill=1.0, base=0,
                               pattern=[[-1, P]], channel_multiplier=1).then_inc(const_p, 1)
            pool.memset(ones[:], 1.0).then_inc(const_p, 1)
            pool.iota(place[:], pattern=[[-1, N]], base=N, channel_multiplier=0,
                      allow_small_or_imprecise_dtypes=True).then_inc(const_p, 1)
            pool.iota(idx_base[:], pattern=[[N, B], [0, TPB]], base=N, channel_multiplier=0,
                      allow_small_or_imprecise_dtypes=True).then_inc(const_p, 1)

            pool.memset(eps_sb[:], EPS).then_inc(const_p, 1)

            def step(i, u):
                t = tile(i, u)
                pool.wait_ge(idx_ready, t + 1)
                pool.wait_ge(gath_free, t + 1)
                pool.sem_inc(gath_begun, 1)
                for k in range(S):
                    pool.indirect_dma_start(
                        out=gath[:, u % 2, k, :], out_offset=None, in_=x_rows,
                        in_offset=bass.IndirectOffsetOnAxis(ap=idx[:, u % 2, k:k + 1], axis=0),
                    ).then_inc(gath_in[u % 2], 16)

            steps(pool, step, NT)

        @block.vector
        def _(dve):
            for _ in range(2):
                dve.sem_inc(adj_free, 1)
                dve.sem_inc(gath_free, 1)
            for _ in range(U):
                dve.sem_inc(x_free, 1)
            dve.wait_ge(const_p, 4)

            def extract(i, u):
                t, b = tile(i, u), u % 2
                n = 0

                def then(ins):
                    nonlocal n
                    n += 1
                    ins.then_inc(dve_step, 1)
                    dve.wait_ge(dve_step, n)

                dve.wait_ge(adj_in[b], 16 * (use(i, u) + 1))
                then(dve.scalar_tensor_tensor(out=score[:], in0=adj_sb[:, b, :], scalar=0.0, in1=place[:],
                                              op0=ALU.not_equal, op1=ALU.mult))
                dve.sem_inc(adj_free, 1)
                for r in range(TOP // 8):
                    eight = top[:, b, 8 * r:8 * r + 8]
                    then(dve.max(out=eight, in_=score[:]))
                    if r < TOP // 8 - 1:
                        then(dve.match_replace(out=score[:], in_to_replace=eight, in_values=score[:], imm_value=0.0))
                then(dve.scalar_tensor_tensor(out=filled[:], in0=top[:, b, :], scalar=0.0,
                                              in1=top[:, b, 0:1].broadcast_to((P, TOP)),
                                              op0=ALU.is_equal, op1=ALU.mult))
                then(dve.tensor_tensor(filled[:], filled[:], top[:, b, :], ALU.add))
                then(dve.tensor_scalar(filled[:], filled[:], 1.0, -1.0, ALU.max, ALU.mult))
                then(dve.tensor_scalar(floor[:, b, 0:1], top[:, b, S:S + 1], 0.0, -BIG, ALU.is_gt, ALU.mult))
                then(dve.tensor_scalar(floor[:, b, 1:2], top[:, b, 0:1], 0.0, BIG, ALU.is_gt, ALU.mult))
                then(dve.tensor_scalar(idx[:, b, :], filled[:], idx_base[:, bass.ds(t, 1)], None, ALU.add))
                dve.sem_inc(idx_ready, 1)
                dve.sem_clear(dve_step)

            def reduce(i, u):
                t, b = tile(i, u), u % 2
                dve.wait_ge(gath_in[b], 16 * S * (use(i, u) + 1))
                dve.wait_ge(y_ready, t + 1)
                dve.tensor_reduce(agg[:, b, :], gath[:, b, :, :].rearrange("p k c -> p c k"), AX_X,
                                  ALU.max).then_inc(gath_free, 1)
                dve.wait_ge(gath_free, t + 3)
                dve.tensor_scalar(agg[:, b, :], agg[:, b, :], floor[:, b, 0:1], floor[:, b, 1:2],
                                  ALU.max, ALU.min).then_inc(agg_ready, 1)

            def residual(i, u):
                t, b = tile(i, u), u % 2
                dve.wait_ge(y_ready, t + 3)
                dve.wait_ge(res_ready, t + 1)
                dve.scalar_tensor_tensor(out=z[:, b, :], in0=ps_y[b][:], scalar=0.0, in1=x_sb[:, u, :],
                                         op0=ALU.max, op1=ALU.add).then_inc(x_free, 1)
                dve.wait_ge(x_free, t + U + 1)
                dve.bn_stats(out=stats[:], in_=z[:, b, :]).then_inc(dve_step, 1)
                dve.wait_ge(dve_step, 1)
                dve.bn_aggr(out=mv[:, b, :], in_=stats[:]).then_inc(dve_step, 1)
                dve.wait_ge(dve_step, 2)
                dve.sem_inc(var_ready, 1)
                dve.sem_clear(dve_step)

            def scales(i, u):
                t, b = tile(i, u), u % 2
                dve.wait_ge(std_ready, t + 1)
                dve.reciprocal(scale[:, b, 0:1], std[:, b:b + 1]).then_inc(dve_step, 1)
                dve.wait_ge(dve_step, 1)
                dve.scalar_tensor_tensor(out=scale[:, b, 1:2], in0=mv[:, b, 0:1], scalar=-1.0,
                                         in1=scale[:, b, 0:1], op0=ALU.mult, op1=ALU.mult).then_inc(dve_step, 1)
                dve.wait_ge(dve_step, 2)
                dve.sem_inc(scale_ready, 1)
                dve.sem_clear(dve_step)

            def step(i, u):
                now, one, two = (lagged(i, u, k) for k in range(3))
                if two:
                    residual(*two)
                if now:
                    extract(*now)
                if one:
                    reduce(*one)
                if two:
                    scales(*two)

            steps(dve, step, LAST)

        @block.scalar
        def _(act):
            for _ in range(2):
                act.sem_inc(res_ready, 1)
                act.sem_inc(hT_ready, 1)

            def columns(i, u):
                t, b = tile(i, u), u % 2
                act.wait_ge(hT_psum, t + 1)
                act.wait_ge(y_ready, t + 1)
                act.copy(hT[:, b, :, :], ps_t[b][:]).then_inc(hT_ready, 1)

            def deviation(i, u):
                t, b = tile(i, u), u % 2
                act.wait_ge(var_ready, t + 1)
                act.activation(std[:, b:b + 1], mv[:, b, 1:2], ACT.Sqrt, bias=eps_sb[:, 0:1]).then_inc(std_ready, 1)

            def normalise(i, u):
                t, b = tile(i, u), u % 2
                act.wait_ge(scale_ready, t + 1)
                if not isinstance(i, int) or i > 0 or u >= 2:
                    act.wait_ge(out_done[b], 16 * use(i, u))
                act.activation(res[:, b, :], z[:, b, :], ACT.Identity, bias=scale[:, b, 1:2],
                               scale=scale[:, b, 0:1]).then_inc(res_ready, 1)
                act.wait_ge(res_ready, t + 3)
                act.dma_start(out_rows[bass.ds(t * P, P), :], res[:, b, :]).then_inc(out_done[b], 16)

            def step(i, u):
                one, two = lagged(i, u, 1), lagged(i, u, 2)
                if two:
                    deviation(*two)
                if one:
                    columns(*one)
                if two:
                    normalise(*two)

            act.wait_ge(const_p, 5)
            steps(act, step, LAST)
            for o in out_done:
                act.wait_ge(o, 16 * NT // 2)

        @block.tensor
        def _(pe):
            for _ in range(2):
                pe.sem_inc(y_ready, 1)
            pe.wait_ge(const_p, 4)
            pe.wait_ge(w_in, 32)

            def step(i, u):
                if lagged(i, u, 1) is None:
                    return
                i, u = lagged(i, u, 1)
                t, b = tile(i, u), u % 2
                pe.wait_ge(hT_ready, t + 1)
                pe.wait_ge(x_in[u], 16 * (i + 1))
                for c in range(KC):
                    pe.transpose(ps_t[b][:, c, :], x_sb[:, u, c * P:(c + 1) * P], ident[:])
                pe.wait_ge(agg_ready, t + 1)
                for c in range(KC):
                    last = pe.transpose(ps_t[b][:, KC + c, :], agg[:, b, c * P:(c + 1) * P], ident[:])
                last.then_inc(hT_psum, 1)
                if not (isinstance(i, int) and i == 0 and u < 2):
                    pe.wait_ge(x_free, t + U - 1)
                pe.matmul(ps_y[b][:], ones[:], bias_sb[:], start=True, stop=False)
                pe.wait_ge(hT_ready, t + 3)
                for c in range(2 * KC):
                    last = pe.matmul(ps_y[b][:], hT[:, b, c, :], w_sb[:, c, :], start=False, stop=(c == 2 * KC - 1))
                last.then_inc(y_ready, 1)

            steps(pe, step, NT + 1)


_INS = ["x", "adj", "L0_gnn_W", "L0_gnn_b"]


def kernel(**inputs):
    import numpy as _np
    import concourse.bacc as _bacc
    from concourse import mybir as _mybir
    from concourse.bass_utils import run_bass_kernel_spmd as _run

    nc = _bacc.Bacc("TRN2", target_bir_lowering=False, num_devices=1)
    arrays, args = {}, []
    for name in _INS:
        a = _np.ascontiguousarray(inputs[name])
        arrays[f"in_{name}_dram"] = a
        args.append(nc.dram_tensor(f"in_{name}_dram", a.shape, _mybir.dt.from_np(a.dtype), kind="ExternalInput").ap())
    shape = tuple(inputs["x"].shape)
    args.append(nc.dram_tensor("out_0_dram", shape, _mybir.dt.float32, kind="ExternalOutput").ap())
    build(nc, *args)
    r = _run(nc, [arrays], core_ids=[0])
    return r.results[0]["out_0_dram"]
```

```python
from contextlib import ExitStack

import concourse.bass as bass
from concourse import mybir
from concourse.alu_op_type import AluOpType as ALU


P = 128
S = 25
MADE = 44
TOP = 32
U = 4
PEELED = 3
L = 2
GB = 2
G = 15
RG = -(-G // 8)
EPS = 1e-5
BIG = 3.0e38
CODE = 64
FLAG_MAX = 1 << 30
FOUND = 32768.0
ECAP = 64

ACT = mybir.ActivationFunctionType
F32 = mybir.dt.float32
BF16 = mybir.dt.bfloat16
I32 = mybir.dt.int32
AX_X = mybir.AxisListType.X
AX_XY = mybir.AxisListType.XY


def build(nc: bass.Bass, x: bass.AP, adj: bass.AP, w: bass.AP, bias: bass.AP, out: bass.AP):
    B, N, C = x.shape
    OUT = w.shape[1]
    NT = B * N // P
    KB = N // P
    KC = C // P
    NQ = KB // 4
    W8 = P // 8
    NW = KB * W8
    NCH = L * KB // GB // 4
    TURNS = KB // U
    LAST = NT + 8

    x_rows = x.rearrange("b n c -> (b n) c")
    adj_rows = adj.rearrange("b n m -> (b n) m")
    out_rows = out.rearrange("b n c -> (b n) c")

    with ExitStack() as ctx:
        def sb(name, shape, dt=F32):
            return ctx.enter_context(nc.sbuf_tensor(name, shape, dt))

        def pb(name, shape, dt=F32):
            return ctx.enter_context(nc.psum_tensor(name, shape, dt))

        def sem(name):
            return ctx.enter_context(nc.semaphore(name))

        def sems(name, n):
            return [sem(f"{name}{k}") for k in range(n)]

        ident = sb("ident", [P, P])
        ident_h = sb("ident_h", [P, P], BF16)
        rank_all = sb("rank_all", [P, P], BF16)
        rank_kept = sb("rank_kept", [P, P], BF16)
        half = sb("half", [P, P], BF16)
        rank_bias = sb("rank_bias", [P, GB])
        left_band = sb("left_band", [P, KB + P], BF16)
        spread = sb("spread", [P, KB, P], BF16)
        in_all_row = sb("in_all_row", [P, 1], BF16)
        word_of = sb("word_of", [P, W8], BF16)
        key_base = sb("key_base", [P, KB, W8])
        bit_value = sb("bit_value", [P, 8], I32)
        bit_place = sb("bit_place", [P, 8])
        idx_base = sb("idx_base", [P, NT])
        ones = sb("ones", [P, P])
        zeros = sb("zeros", [P, 1])
        above_edge = sb("above_edge", [P, 1])
        eps_sb = sb("eps_sb", [P, 1])
        kept_edge = sb("kept_edge", [P, 1])
        ecap_sb = sb("ecap_sb", [P, 1])
        w_sb = sb("w_sb", [P, 2 * KC, OUT])
        bias_sb = sb("bias_sb", [1, OUT])

        adj_sb = sb("adj_sb", [P, 2, N], I32)
        sign_sb = sb("sign_sb", [P, N], BF16)
        mask = sb("mask", [P, KB, P], BF16)
        left = sb("left", [P, P], BF16)
        kept = sb("kept", [P, KB, P], BF16)
        rank = sb("rank", [P, KB, P], BF16)
        pick = sb("pick", [P, 2, L, KB, P], BF16)
        rest = sb("rest", [P, KB, P], BF16)

        xp = sb("xp", [P, KB, 3, C], BF16)
        xp_next = sb("xp_next", [P, KB, 3, C], BF16)
        x_piece = sb("x_piece", [P, 2, C])
        left_over = sb("left_over", [P, C])
        x_sb = sb("x_sb", [P, U, C])

        key = sb("key", [P, KB, W8])
        words = sb("words", [P, 8 * RG])
        words_i = sb("words_i", [P, 8 * RG], I32)
        bit_set = sb("bit_set", [P, 8 * RG, 8], I32)
        word_place = sb("word_place", [P, 8 * RG], I32)
        cand = sb("cand", [P, 8 * RG, 8])
        found = sb("found", [P, U, 8 * RG])
        idx = sb("idx", [P, 2, 8 * RG], I32)
        rows = sb("rows", [P, 2, G + NCH, C])
        above = sb("above", [P, U])
        row_max = sb("row_max", [P, C])
        least = sb("least", [P, 1])
        doubt = sb("doubt", [P, 2, U])
        again = sb("again", [1, 2], I32)
        agg = sb("agg", [P, U, C])

        score = sb("score", [P, N], I32)
        score_f = score[:].bitcast(F32)
        top = sb("top", [P, TOP])
        filled = sb("filled", [P, TOP])
        idx_all = sb("idx_all", [P, TOP], I32)
        floor = sb("floor", [P, 2])
        rows_all = sb("rows_all", [P, S, C])
        place = rows_all[:, 0:N // C, :].rearrange("p k c -> p (k c)")

        hT = sb("hT", [P, 2 * KC, P])
        z = sb("z", [P, 2, OUT])
        stats = sb("stats", [P, 6])
        mv = sb("mv", [P, 2, 2])
        std = sb("std", [P, 2])
        scale = sb("scale", [P, 2, 2])
        res = sb("res", [P, 2, OUT])

        ps_pick = [pb(f"ps_pick{k}", [P, 4, C]) for k in range(2)]
        ps_work = [pb(f"ps_work{k}", [P, 4 * P]) for k in range(3)]
        ORDER = ("mask0", "mask1", "hT", "row0", "row1", "row2", "row3", "group0", "group1", "group2", "group3", "y")
        bank = {name: ps_work[k % 3] for k, name in enumerate(ORDER)}
        ps_mask = [bank[f"mask{h}"][:].bitcast(BF16).rearrange("p (k r) -> p k r", k=8) for h in range(2)]
        ps_row = [bank[f"row{q}"][:].rearrange("p (k r) -> p k r", k=4) for q in range(NQ)]
        ps_group = [bank[f"group{q}"][:].rearrange("p (k r) -> p k r", k=4) for q in range(NQ)]
        ps_hT = bank["hT"][:].rearrange("p (k r) -> p k r", k=4)
        ps_y = bank["y"][:, 0:OUT]
        ps_misc = pb("ps_misc", [P, 512])
        n_words = KB * W8
        ps_words = ps_misc[:, 0:n_words].rearrange("p (k w) -> p k w", k=KB)
        ps_left = ps_misc[:, n_words:n_words + P]
        ps_count = ps_misc[:, n_words + P:n_words + P + 1]
        ps_again = ps_misc[0:1, n_words + P + 2:n_words + P + 2 + U]

        adj_in = sems("adj_in", 2)
        piece_in = sems("piece_in", 2)
        x_in = sems("x_in", U)
        w_in = sem("w_in")
        first_in = sem("first_in")
        rows_in = sems("rows_in", 2)
        out_done = sems("out_done", 2)
        constants = sem("constants")
        halves = sem("halves")
        sign_done = sem("sign_done")
        mask_t = sems("mask_t", 2)
        mask_done = sems("mask_done", 2)
        left_sum = sem("left_sum")
        left_done = sem("left_done")
        rank_sum = sems("rank_sum", NQ)
        kept_done = sems("kept_done", NQ)
        code_sum = sems("code_sum", NQ)
        rank_done = sems("rank_done", NQ)
        pick_done = sem("pick_done")
        words_sum = sem("words_sum")
        words_read = sem("words_read")
        above_done = sem("above_done")
        chunk_done = sems("chunk_done", NCH)
        chunk_max = sems("chunk_max", NCH)
        zeroed = sem("zeroed")
        idx_ready = sem("idx_ready")
        gather_begun = sem("gather_begun")
        cut_begun = sem("cut_begun")
        redo_begun = sem("redo_begun")
        reduced = sem("reduced")
        doubt_ready = sem("doubt_ready")
        again_sum = sem("again_sum")
        again_ready = sem("again_ready")
        reviewed = sem("reviewed")
        all_adj_in = sem("all_adj_in")
        place_ready = sem("place_ready")
        all_idx_ready = sem("all_idx_ready")
        all_rows_in = sem("all_rows_in")
        all_reduced = sem("all_reduced")
        parts_done = sem("parts_done")
        xp_ready = sem("xp_ready")
        hT_sum = sem("hT_sum")
        hT_done = sem("hT_done")
        y_sum = sem("y_sum")
        residual_done = sem("residual_done")
        std_done = sem("std_done")
        scale_done = sem("scale_done")
        res_done = sem("res_done")
        dve_step = sem("dve_step")
        pool_step = sem("pool_step")

        block = ctx.enter_context(nc.Block())

        def steps(eng, step, last=LAST):
            for s in range(KB):
                step(s // U, s % U, None)
            with eng.Fori(1, B) as g:
                for u in range(U):
                    step(TURNS * g, u, g)
                with eng.Fori(1, TURNS) as k:
                    for u in range(U):
                        step(TURNS * g + k, u, None)
            for s in range(NT, last):
                step(s // U, s % U, None)

        def flat_steps(eng, step, last=LAST):
            for s in range(PEELED * U):
                step(s // U, s % U)
            with eng.Fori(PEELED, NT // U) as i:
                for u in range(U):
                    step(i, u)
            for s in range(NT, last):
                step(s // U, s % U)

        def lagged(i, u, lag):
            if isinstance(i, int):
                t = U * i + u - lag
                return divmod(t, U) if 0 <= t < NT else None
            return i + (u - lag) // U, (u - lag) % U

        def done(eng, sm, t, ago=0):
            if not isinstance(t, int) or t >= ago:
                eng.wait_ge(sm, t - ago + 1)

        def used(i, u):
            return U // 2 * i + u // 2

        @block.sync
        def _(sp):
            sp.dma_start(w_sb[:], w.rearrange("(k p) o -> p k o", p=P)).then_inc(w_in, 16)
            sp.dma_start(bias_sb[:], bias.rearrange("(a o) -> a o", a=1)).then_inc(w_in, 16)

            sp.dma_start(rows_all[:, 0:KB, :], x[0].rearrange("(k p) c -> p k c", p=P)).then_inc(first_in, 16)

            def load_adj(i, u):
                t, b = U * i + u, u % 2
                done(sp, sign_done, t, 2)
                sp.dma_start(adj_sb[:, b, :], adj_rows[bass.ds(t * P, P), :]).then_inc(adj_in[b], 16)

            def load_piece(i, u):
                t, b = U * i + u, u % 2
                done(sp, parts_done, t, 2)
                sp.dma_start(x_piece[:, b, :], x_rows[bass.ds((t + KB) * P, P), :]).then_inc(piece_in[b], 16)

            def load_x(i, u):
                t = U * i + u
                done(sp, residual_done, t, U)
                sp.dma_start(x_sb[:, u, :], x_rows[bass.ds(t * P, P), :]).then_inc(x_in[u], 16)

            def step(i, u, pieces=True):
                if lagged(i, u, 0):
                    load_adj(i, u)
                    if pieces:
                        load_piece(i, u)
                own = lagged(i, u, 6)
                if own:
                    load_x(*own)

            for s in range(PEELED * U):
                step(s // U, s % U)
            with sp.Fori(PEELED, NT // U - TURNS) as i:
                for u in range(U):
                    step(i, u)
            with sp.Fori(NT // U - TURNS, NT // U) as i:
                for u in range(U):
                    step(i, u, False)
            for s in range(NT, NT + 6):
                step(s // U, s % U, False)

        @block.gpsimd
        def _(pool):
            made = 0

            def then(ins):
                nonlocal made
                made += 1
                ins.then_inc(constants, 1)
                pool.wait_ge(constants, made)

            def select(ap, pattern, op, fill, base=0, cm=0):
                then(pool.affine_select(out=ap, in_=ap, pattern=pattern, compare_op=op, fill=fill, base=base,
                                        channel_multiplier=cm))

            for m in (ident, ident_h):
                then(pool.memset(m[:], 0.0))
                select(m[:], [[-1, P]], ALU.not_equal, 1.0, cm=1)
            for m, one, diag in ((rank_all, 1.0, 1.0 - 4 * CODE), (rank_kept, 0.5, 0.5 + CODE)):
                then(pool.memset(m[:], one))
                select(m[:], [[1, P]], ALU.is_ge, 0.0, cm=-1)
                select(m[:], [[-1, P]], ALU.not_equal, diag, cm=1)
            then(pool.memset(half[:], 0.5))
            then(pool.memset(left_band[:, 0:KB + 1], 0.0))
            then(pool.memset(left_band[:, KB + 1:KB + P], 1.0))
            then(pool.memset(spread[:], -1.0))
            select(spread[:], [[-1, KB], [0, P]], ALU.is_equal, 0.0, cm=1)
            then(pool.memset(in_all_row[:], 1.0))
            select(in_all_row[:], [[0, 1]], ALU.is_equal, 0.0, base=-KB, cm=1)
            then(pool.memset(word_of[:], 0.0))
            for k in range(8):
                select(word_of[:], [[-8, W8]], ALU.not_equal, float(2 ** k), base=-k, cm=1)
                then(pool.memset(bit_value[:, k:k + 1], 2 ** k))
            for ap, pattern, base, cm in ((key_base[:], [[-256, NW]], 256 * NW, 0), (bit_place[:], [[1, 8]], -int(FOUND), 0),
                                          (idx_base[:], [[N, B], [0, KB]], N + int(FOUND), 0),
                                          (rank_bias[:], [[P, GB]], 1, 1)):
                then(pool.iota(ap, pattern=pattern, base=base, channel_multiplier=cm,
                               allow_small_or_imprecise_dtypes=True))
            for ap, value in ((ones[:], 1.0), (zeros[:], 0.0), (eps_sb[:], EPS), (above_edge[:], float(ECAP - S)), (ecap_sb[:], float(ECAP)),
                              (kept_edge[:], S - 4 * CODE - ECAP + 0.5)):
                then(pool.memset(ap, value))
            assert made == MADE, made

            def cut(i, u, k):
                t, b = U * i + u, u % 2
                n = 0

                def then(ins):
                    nonlocal n
                    n += 1
                    ins.then_inc(pool_step, 1)
                    pool.wait_ge(pool_step, n)

                pool.wait_ge(piece_in[b], 16 * (used(i, u) + 1))
                pool.sem_inc(cut_begun, 1)
                part = [xp_next[:, bass.ds(U * k + u, 1), q, :].rearrange("p a c -> p (a c)") for q in range(3)]
                then(pool.tensor_copy(part[0], x_piece[:, b, :]))
                then(pool.tensor_tensor(left_over[:], x_piece[:, b, :], part[0], ALU.subtract))
                then(pool.tensor_copy(part[1], left_over[:]))
                then(pool.tensor_tensor(left_over[:], left_over[:], part[1], ALU.subtract))
                then(pool.tensor_copy(part[2], left_over[:]))
                pool.sem_inc(parts_done, 1)
                pool.sem_clear(pool_step)

            def gather(i, u):
                t, b = U * i + u, u % 2
                done(pool, idx_ready, t)
                done(pool, zeroed, t)
                pool.sem_inc(gather_begun, 1)
                for k in range(G):
                    pool.indirect_dma_start(
                        out=rows[:, b, k, :], out_offset=None, in_=x_rows,
                        in_offset=bass.IndirectOffsetOnAxis(ap=idx[:, b, k:k + 1], axis=0),
                        bounds_check=B * N - 1, oob_is_err=False,
                    ).then_inc(rows_in[b], 16)

            def redo(i):
                pool.wait_ge(again_ready, i + 1)
                pool.sem_inc(redo_begun, 1)
                flag = pool.value_load(again[0:1, 0:1], min_val=0, max_val=FLAG_MAX)
                with pool.If(flag > 0):
                    for u in range(U):
                        t = U * i + u
                        if u > 0:
                            pool.wait_ge(all_reduced, t)
                            pool.sem_inc(redo_begun, 1)
                        pool.iota(place, pattern=[[-1, N]], base=N, channel_multiplier=0,
                                  allow_small_or_imprecise_dtypes=True).then_inc(place_ready, 1)
                        pool.dma_start(score[:], adj_rows[bass.ds(t * P, P), :]).then_inc(all_adj_in, 16)
                        pool.wait_ge(all_idx_ready, t + 1)
                        pool.sem_inc(redo_begun, 1)
                        for k in range(S):
                            pool.indirect_dma_start(
                                out=rows_all[:, k, :], out_offset=None, in_=x_rows,
                                in_offset=bass.IndirectOffsetOnAxis(ap=idx_all[:, k:k + 1], axis=0),
                            ).then_inc(all_rows_in, 16)
                with pool.Else():
                    pool.inc_swdge_sem([all_adj_in], [16 * U])
                    pool.inc_swdge_sem([all_rows_in], [16 * S * U])
                pool.wait_ge(reviewed, i + 1)

            def step(i, u, k=None, g=0):
                if u == U - 1 and lagged(i, 0, U):
                    redo(i - 1)
                two = lagged(i, u, 2)
                if two:
                    gather(*two)
                if k is not None:
                    if u == 0:
                        pool.wait_ge(xp_ready, g + 1)
                    cut(i, u, k)

            for u in range(U):
                step(0, u, 0)
            with pool.Fori(1, TURNS) as k:
                for u in range(U):
                    step(k, u, k)
            with pool.Fori(1, B - 1) as g:
                with pool.Fori(0, TURNS) as k:
                    for u in range(U):
                        step(TURNS * g + k, u, k, g)
            with pool.Fori(NT // U - TURNS, NT // U) as i:
                for u in range(U):
                    step(i, u)
            for s in range(NT, LAST):
                step(s // U, s % U)

        @block.vector
        def _(dve):
            dve.wait_ge(constants, MADE)
            dve.tensor_scalar(rank_bias[:], rank_bias[:], 0.5, None, ALU.mult).then_inc(halves, 1)

            n = 0

            def then(ins):
                nonlocal n
                n += 1
                ins.then_inc(dve_step, 1)
                dve.wait_ge(dve_step, n)

            def free(ins):
                nonlocal n
                n += 1
                ins.then_inc(dve_step, 1)

            def fresh():
                nonlocal n
                dve.sem_clear(dve_step)
                n = 0

            first = rows_all[:, 0:KB, :]
            dve.wait_ge(first_in, 16)
            then(dve.tensor_copy(xp[:, :, 0, :], first))
            then(dve.tensor_tensor(first, first, xp[:, :, 0, :], ALU.subtract))
            then(dve.tensor_copy(xp[:, :, 1, :], first))
            then(dve.tensor_tensor(first, first, xp[:, :, 1, :], ALU.subtract))
            then(dve.tensor_copy(xp[:, :, 2, :], first))
            dve.sem_inc(xp_ready, 1)
            fresh()

            def new_parts(g):
                dve.wait_ge(parts_done, KB * g)
                dve.wait_ge(chunk_done[NCH - 1], KB * g)
                then(dve.tensor_copy(xp[:], xp_next[:]))
                dve.sem_inc(xp_ready, 1)
                fresh()

            def selects(i, u):
                t, b = U * i + u, u % 2
                done(dve, rank_done[NQ - 1], t)
                for q in range(L):
                    free(dve.tensor_scalar(pick[:, b, q, :, :], rank[:], float(CODE + 1 + q), None, ALU.is_equal))
                then(dve.tensor_scalar(rest[:], rank[:], float(CODE + 1 + L), None, ALU.is_ge))
                dve.sem_inc(pick_done, 1)
                fresh()

            def extract(i, u):
                t, b = U * i + u, u % 2
                done(dve, words_sum, t)
                then(dve.scalar_tensor_tensor(out=key[:], in0=ps_words, scalar=0.0, in1=key_base[:],
                                              op0=ALU.is_gt, op1=ALU.mult))
                then(dve.tensor_tensor(key[:], ps_words, key[:], ALU.add))
                dve.sem_inc(words_read, 1)
                for r in range(RG):
                    eight = words[:, 8 * r:8 * r + 8]
                    then(dve.max(out=eight, in_=key[:]))
                    if r < RG - 1:
                        then(dve.match_replace(out=key[:], in_to_replace=eight, in_values=key[:], imm_value=0.0))
                then(dve.tensor_copy(words_i[:], words[:]))
                shape = (P, 8 * RG, 8)
                free(dve.tensor_tensor(bit_set[:], words_i[:].unsqueeze(2).broadcast_to(shape),
                                       bit_value[:].unsqueeze(1).broadcast_to(shape), ALU.bitwise_and))
                then(dve.tensor_scalar(word_place[:], words_i[:], -256, None, ALU.bitwise_and))
                then(dve.scalar_tensor_tensor(out=cand[:], in0=word_place[:].unsqueeze(2).broadcast_to(shape),
                                              scalar=1.0 / 32.0, in1=bit_place[:].unsqueeze(1).broadcast_to(shape),
                                              op0=ALU.mult, op1=ALU.subtract))
                then(dve.scalar_tensor_tensor(out=cand[:], in0=bit_set[:], scalar=0.0, in1=cand[:],
                                              op0=ALU.is_gt, op1=ALU.mult))
                for r in range(RG):
                    eight = found[:, u, 8 * r:8 * r + 8]
                    then(dve.max(out=eight, in_=cand[:]))
                    if r < RG - 1:
                        then(dve.match_replace(out=cand[:], in_to_replace=eight, in_values=cand[:], imm_value=0.0))
                then(dve.tensor_scalar(idx[:, b, :], found[:, u, :], -1.0, idx_base[:, bass.ds(t, 1)],
                                       ALU.mult, ALU.add))
                dve.sem_inc(idx_ready, 1)
                fresh()

            def chunk(i, u, c):
                t, b = U * i + u, u % 2
                done(dve, chunk_done[c], t)
                dve.tensor_reduce(rows[:, b, G + c, :], ps_pick[c % 2][:].rearrange("p o c -> p c o"), AX_X,
                                  ALU.max).then_inc(chunk_max[c], 1)

            def reduce(i, u):
                t, b = U * i + u, u % 2
                dve.wait_ge(rows_in[b], 16 * G * (used(i, u) + 1))
                done(dve, chunk_max[NCH - 1], t)
                done(dve, hT_sum, t, U)
                then(dve.tensor_reduce(row_max[:], rows[:, b, :, :].rearrange("p k c -> p c k"), AX_X, ALU.max))
                dve.sem_inc(reduced, 1)
                then(dve.tensor_scalar(agg[:, u, :], row_max[:], 0.0, None, ALU.max, ALU.min, accum_out=least[:]))
                done(dve, above_done, t)
                then(dve.scalar_tensor_tensor(out=least[:], in0=least[:], scalar=0.0, in1=above[:, u:u + 1],
                                              op0=ALU.is_le, op1=ALU.mult))
                then(dve.tensor_tensor(doubt[:, 0, u:u + 1], least[:], found[:, u, G:G + 1], ALU.max))
                if u == U - 1:
                    dve.sem_inc(doubt_ready, 1)
                fresh()

            def redo(i, u):
                t = U * i + u
                dve.wait_ge(all_adj_in, 16 * (t + 1))
                dve.wait_ge(place_ready, t + 1)
                then(dve.scalar_tensor_tensor(out=score_f, in0=score[:], scalar=0.0, in1=place,
                                              op0=ALU.not_equal, op1=ALU.mult))
                for r in range(TOP // 8):
                    eight = top[:, 8 * r:8 * r + 8]
                    then(dve.max(out=eight, in_=score_f))
                    if r < TOP // 8 - 1:
                        then(dve.match_replace(out=score_f, in_to_replace=eight, in_values=score_f, imm_value=0.0))
                then(dve.scalar_tensor_tensor(out=filled[:], in0=top[:], scalar=0.0,
                                              in1=top[:, 0:1].broadcast_to((P, TOP)),
                                              op0=ALU.is_equal, op1=ALU.mult))
                then(dve.tensor_tensor(filled[:], filled[:], top[:], ALU.add))
                then(dve.tensor_scalar(filled[:], filled[:], 1.0, -1.0, ALU.max, ALU.mult))
                then(dve.tensor_scalar(floor[:, 0:1], top[:, S:S + 1], 0.0, -BIG, ALU.is_gt, ALU.mult))
                then(dve.tensor_scalar(floor[:, 1:2], top[:, 0:1], 0.0, BIG, ALU.is_gt, ALU.mult))
                then(dve.tensor_scalar(idx_all[:], filled[:], idx_base[:, bass.ds(t, 1)], -FOUND, ALU.add, ALU.add))
                dve.sem_inc(all_idx_ready, 1)
                dve.wait_ge(all_rows_in, 16 * S * (t + 1))
                then(dve.tensor_reduce(row_max[:], rows_all[:].rearrange("p k c -> p c k"), AX_X, ALU.max))
                dve.sem_inc(all_reduced, 1)
                then(dve.tensor_scalar(agg[:, u, :], row_max[:], floor[:, 0:1], floor[:, 1:2], ALU.max, ALU.min))
                fresh()

            def review(i):
                dve.wait_ge(again_sum, i + 1)
                then(dve.tensor_reduce(again[:, 0:1], ps_again, AX_X, ALU.max))
                dve.sem_inc(again_ready, 1)
                flag = dve.value_load(again[0:1, 0:1], min_val=0, max_val=FLAG_MAX)
                fresh()
                with dve.If(flag > 0):
                    for u in range(U):
                        redo(i, u)
                with dve.Else():
                    dve.sem_inc(place_ready, U)
                    dve.sem_inc(all_idx_ready, U)
                    dve.sem_inc(all_reduced, U)
                dve.sem_inc(reviewed, 1)

            def residual(i, u):
                t, b = U * i + u, u % 2
                done(dve, y_sum, t)
                done(dve, res_done, t, 2)
                then(dve.scalar_tensor_tensor(out=z[:, b, :], in0=ps_y, scalar=0.0,
                                              in1=x_sb[:, u, :], op0=ALU.max, op1=ALU.add))
                then(dve.bn_stats(out=stats[:], in_=z[:, b, :]))
                then(dve.bn_aggr(out=mv[:, b, :], in_=stats[:]))
                dve.sem_inc(residual_done, 1)
                fresh()

            def scales(i, u):
                t, b = U * i + u, u % 2
                done(dve, std_done, t)
                then(dve.reciprocal(scale[:, b, 0:1], std[:, b:b + 1]))
                then(dve.scalar_tensor_tensor(out=scale[:, b, 1:2], in0=mv[:, b, 0:1], scalar=-1.0,
                                              in1=scale[:, b, 0:1], op0=ALU.mult, op1=ALU.mult))
                dve.sem_inc(scale_done, 1)
                fresh()

            def step(i, u, graph):
                one, two, three, eight = (lagged(i, u, k) for k in (1, 2, 3, 8))
                if graph is not None and u == 2:
                    new_parts(graph)
                if eight:
                    residual(*eight)
                if u == U - 1 and lagged(i, 0, U):
                    review(i - 1)
                if two:
                    extract(*two)
                    for c in range(NCH // 2):
                        chunk(*two, c)
                if eight:
                    scales(*eight)
                if three:
                    reduce(*three)
                if two:
                    for c in range(NCH // 2, NCH - 1):
                        chunk(*two, c)
                if one:
                    selects(*one)
                if two:
                    chunk(*two, NCH - 1)

            steps(dve, step)

        @block.scalar
        def _(act):
            act.wait_ge(halves, 1)

            def signs(i, u):
                t, b = U * i + u, u % 2
                act.wait_ge(adj_in[b], 16 * (used(i, u) + 1))
                done(act, mask_t[1], t, 1)
                act.activation(sign_sb[:], adj_sb[:, b, :], ACT.Sign).then_inc(sign_done, 1)

            def masks(i, u):
                t = U * i + u
                if not isinstance(t, int) or t > 0:
                    act.wait_ge(rank_sum[NQ - 1], t)
                for h in range(2):
                    done(act, mask_t[h], t)
                    act.activation(mask[:, 8 * h:8 * h + 8, :], ps_mask[h], ACT.Square).then_inc(mask_done[h], 1)

            def lefts(i, u):
                t = U * i + u
                done(act, left_sum, t)
                act.activation(left[:], ps_left, ACT.Relu, scale=-1.0,
                               bias=ecap_sb[:, 0:1]).then_inc(left_done, 1)

            def keeps(i, u):
                t = U * i + u
                for q in range(NQ):
                    done(act, rank_sum[q], t)
                    if q == 0:
                        done(act, code_sum[NQ - 1], t, 1)
                    act.activation(kept[:, 4 * q:4 * q + 4, :], ps_row[q], ACT.Sign, scale=-1.0,
                                   bias=kept_edge[:, 0:1]).then_inc(kept_done[q], 1)

            def ranks(i, u):
                t = U * i + u
                for q in range(NQ):
                    done(act, code_sum[q], t)
                    if q == 0:
                        done(act, pick_done, t, 1)
                    for k in range(GB):
                        last = act.activation(rank[:, 4 * q + k:4 * q + 4:GB, :], ps_group[q][:, k::GB, :],
                                              ACT.Identity, bias=rank_bias[:, k:k + 1])
                        if k == GB - 1:
                            last.then_inc(rank_done[q], 1)

            def aboves(i, u):
                t = U * i + u
                done(act, words_read, t)
                act.activation(above[:, u:u + 1], ps_count, ACT.Relu, scale=-1.0,
                               bias=above_edge[:, 0:1]).then_inc(above_done, 1)

            def zero_rows(i, u):
                t, b = U * i + u, u % 2
                done(act, reduced, t, 2)
                act.activation(rows[:, b, 0:G, :].rearrange("p k c -> p (k c)"), zeros[:].broadcast_to((P, G * C)),
                               ACT.Copy).then_inc(zeroed, 1)

            def columns(i, u):
                t = U * i + u
                done(act, hT_sum, t)
                done(act, y_sum, t, 1)
                act.copy(hT[:], ps_hT).then_inc(hT_done, 1)

            def deviation(i, u):
                t, b = U * i + u, u % 2
                done(act, residual_done, t)
                act.activation(std[:, b:b + 1], mv[:, b, 1:2], ACT.Sqrt, bias=eps_sb[:, 0:1]).then_inc(std_done, 1)

            def normalise(i, u):
                t, b = U * i + u, u % 2
                done(act, scale_done, t)
                if not isinstance(i, int) or U * i + u >= 2:
                    act.wait_ge(out_done[b], 16 * used(i, u))
                act.activation(res[:, b, :], z[:, b, :], ACT.Identity, bias=scale[:, b, 1:2],
                               scale=scale[:, b, 0:1]).then_inc(res_done, 1)
                done(act, res_done, t)
                act.dma_start(out_rows[bass.ds(t * P, P), :], res[:, b, :]).then_inc(out_done[b], 16)

            def step(i, u):
                now, one, two, seven, eight, nine = (lagged(i, u, k) for k in (0, 1, 2, 7, 8, 9))
                if one:
                    masks(*one)
                if two:
                    aboves(*two)
                if eight:
                    deviation(*eight)
                if one:
                    lefts(*one)
                if seven:
                    columns(*seven)
                if one:
                    keeps(*one)
                if nine:
                    normalise(*nine)
                if one:
                    ranks(*one)
                if now:
                    signs(*now)
                if one:
                    zero_rows(*one)

            flat_steps(act, step, LAST + 1)
            for o in out_done:
                act.wait_ge(o, 16 * NT // 2)

        @block.tensor
        def _(pe):
            pe.wait_ge(constants, MADE)
            pe.wait_ge(w_in, 32)
            pe.wait_ge(xp_ready, 1)

            def flip(i, u):
                t = U * i + u
                done(pe, sign_done, t)
                for h in range(2):
                    done(pe, rank_done[2 + h], t, 1)
                    for k in range(8):
                        c = 8 * h + k
                        last = pe.transpose(ps_mask[h][:, k, :], sign_sb[:, c * P:(c + 1) * P], ident_h[:])
                    last.then_inc(mask_t[h], 1)

            def count_left(i, u):
                t = U * i + u
                done(pe, words_read, t, 1)
                done(pe, above_done, t, 1)
                for c in range(KB):
                    if c % 8 == 0:
                        done(pe, mask_done[c // 8], t)
                    last = pe.matmul(ps_left, left_band[:, KB - c:KB - c + P], mask[:, c, :], start=(c == 0), stop=(c == KB - 1))
                last.then_inc(left_sum, 1)

            def rank_in_row(i, u, q):
                t = U * i + u
                if q == 0:
                    done(pe, left_done, t)
                elif q == 2:
                    if not isinstance(t, int) or t >= 6:
                        pe.wait_ge(hT_done, t - 5)
                    else:
                        done(pe, rank_done[1], t, 1)
                elif q == 3:
                    done(pe, kept_done[0], t)
                pe.matmul(ps_row[q], rank_all[:], mask[:, 4 * q:4 * q + 4, :], start=True, stop=False)
                for k in range(4):
                    last = pe.matmul(ps_row[q][:, k, :], spread[:, 4 * q + k, :], left[:], start=False, stop=(k == 3))
                last.then_inc(rank_sum[q], 1)

            def rank_in_group(i, u, q):
                t = U * i + u
                done(pe, kept_done[q], t)
                if q < 3:
                    done(pe, kept_done[q + 1], t)
                else:
                    done(pe, rank_done[0], t)
                last = pe.matmul(ps_group[q], rank_kept[:], kept[:, 4 * q:4 * q + 4, :], start=True, stop=(GB == 1))
                more = [(m + k, m + j) for k in range(1, GB) for j in range(k) for m in range(0, 4, GB)]
                for n, (to, of) in enumerate(more):
                    last = pe.matmul(ps_group[q][:, to, :], half[:], kept[:, 4 * q + of, :],
                                     start=False, stop=(n == len(more) - 1))
                last.then_inc(code_sum[q], 1)

            def word_sums(i, u):
                t = U * i + u
                done(pe, pick_done, t)
                done(pe, left_done, t)
                for c in range(KB):
                    pe.matmul(ps_words[:, c, :], rest[:, c, :], word_of[:], start=True, stop=True)
                pe.matmul(ps_count, left[:], in_all_row[:], start=True, stop=True).then_inc(words_sum, 1)

            def picks(i, u, c):
                t, b = U * i + u, u % 2
                if c < 2:
                    done(pe, chunk_max[NCH - 2 + c], t, 1)
                else:
                    done(pe, chunk_max[c - 2], t)
                for o in range(4):
                    q, grp = divmod(4 * c + o, KB // GB)
                    for k in range(GB):
                        for part in range(3):
                            last = pe.matmul(ps_pick[c % 2][:, o, :], pick[:, b, q, GB * grp + k, :],
                                             xp[:, GB * grp + k, part, :], start=(k == 0 and part == 0),
                                             stop=(k == GB - 1 and part == 2))
                last.then_inc(chunk_done[c], 1)

            def doubts(i):
                pe.wait_ge(doubt_ready, i + 1)
                pe.matmul(ps_again, ones[:, 0:1], doubt[:, 0, :], start=True, stop=True).then_inc(again_sum, 1)

            def turn_h(i, u):
                t = U * i + u
                pe.wait_ge(x_in[u], 16 * (i + 1))
                if u == 0:
                    pe.wait_ge(reviewed, i + 1)
                done(pe, residual_done, t, 1)
                if isinstance(t, int) and t == 0:
                    pe.wait_ge(rank_done[1], 6)
                for c in range(KC):
                    pe.transpose(ps_hT[:, c, :], x_sb[:, u, c * P:(c + 1) * P], ident[:])
                for c in range(KC):
                    last = pe.transpose(ps_hT[:, KC + c, :], agg[:, u, c * P:(c + 1) * P], ident[:])
                last.then_inc(hT_sum, 1)

            def output(i, u):
                t = U * i + u
                done(pe, hT_done, t)
                if not isinstance(t, int) or t + 6 < NT:
                    pe.wait_ge(rank_done[1], t + 7)
                pe.matmul(ps_y, ones[0:1, :], bias_sb[:], start=True, stop=False)
                for c in range(2 * KC):
                    last = pe.matmul(ps_y, hT[:, c, :], w_sb[:, c, :], start=False, stop=(c == 2 * KC - 1))
                last.then_inc(y_sum, 1)

            def step(i, u, graph):
                one, two, seven = (lagged(i, u, k) for k in (1, 2, 7))
                if two:
                    if u == U - 1 and lagged(i, 0, U):
                        pe.wait_ge(again_ready, i)
                    word_sums(*two)
                if one:
                    flip(*one)
                if graph is not None and u == 2:
                    pe.wait_ge(xp_ready, graph + 1)
                for c in range(NCH):
                    quarter = c * 4 // NCH if c * 4 % NCH == 0 else None
                    if quarter == 1:
                        if one:
                            count_left(*one)
                        if seven:
                            turn_h(*seven)
                    if quarter == 2 and one:
                        for q in range(NQ):
                            rank_in_row(*one, q)
                    if quarter == 3 and one:
                        for q in range(NQ):
                            rank_in_group(*one, q)
                    if two:
                        picks(*two, c)
                if seven:
                    output(*seven)
                if u == 2 and lagged(i, 0, U):
                    doubts(i - 1)

            steps(pe, step)


_INS = ["x", "adj", "L0_gnn_W", "L0_gnn_b"]


def kernel(**inputs):
    import numpy as _np
    import concourse.bacc as _bacc
    from concourse import mybir as _mybir
    from concourse.bass_utils import run_bass_kernel_spmd as _run

    nc = _bacc.Bacc("TRN2", target_bir_lowering=False, num_devices=1)
    arrays, args = {}, []
    for name in _INS:
        a = _np.ascontiguousarray(inputs[name])
        arrays[f"in_{name}_dram"] = a
        args.append(nc.dram_tensor(f"in_{name}_dram", a.shape, _mybir.dt.from_np(a.dtype), kind="ExternalInput").ap())
    shape = tuple(inputs["x"].shape)
    args.append(nc.dram_tensor("out_0_dram", shape, _mybir.dt.float32, kind="ExternalOutput").ap())
    build(nc, *args)
    r = _run(nc, [arrays], core_ids=[0])
    return r.results[0]["out_0_dram"]
```

```python
from contextlib import ExitStack

import concourse.bass as bass
from concourse import mybir
from concourse.alu_op_type import AluOpType as ALU


P = 128
S = 25
MADE_FIRST = 17
MADE = 46
TOP = 32
U = 4
PEELED = 3
L = 2
GB = 2
SINGLES = 4
G = 15
RG = G // 8 + 1
EPS = 1e-5
BIG = 3.0e38
CODE = 64
FLAG_MAX = 1 << 30
FOUND = 32768.0
ECAP = 64

ACT = mybir.ActivationFunctionType
F32 = mybir.dt.float32
BF16 = mybir.dt.bfloat16
I32 = mybir.dt.int32
AX_X = mybir.AxisListType.X


def build(nc: bass.Bass, x: bass.AP, adj: bass.AP, w: bass.AP, bias: bass.AP, out: bass.AP):
    B, N, C = x.shape
    OUT = w.shape[1]
    NT = B * N // P
    KB = N // P
    KC = C // P
    NQ = KB // 4
    W8 = P // 8
    NW = KB * W8
    PAIRED = KB - SINGLES
    PICKED = [(q, range(k, k + GB)) for q in range(L) for k in range(0, PAIRED, GB)]
    PICKED += [(L - 1, range(k, k + 1)) for k in range(PAIRED, KB)]
    NCH = len(PICKED) // 4
    assert SINGLES == KB // NQ and len(PICKED) % 4 == 0
    TURNS = KB // U
    LAST = NT + 8

    x_rows = x.rearrange("b n c -> (b n) c")
    adj_rows = adj.rearrange("b n m -> (b n) m")
    out_rows = out.rearrange("b n c -> (b n) c")

    with ExitStack() as ctx:
        def sb(name, shape, dt=F32):
            return ctx.enter_context(nc.sbuf_tensor(name, shape, dt))

        def pb(name, shape, dt=F32):
            return ctx.enter_context(nc.psum_tensor(name, shape, dt))

        def sem(name):
            return ctx.enter_context(nc.semaphore(name))

        def sems(name, n):
            return [sem(f"{name}{k}") for k in range(n)]

        ident = sb("ident", [P, P])
        ident_h = sb("ident_h", [P, P], BF16)
        rank_all = sb("rank_all", [P, P], BF16)
        rank_kept = sb("rank_kept", [P, P], BF16)
        half = sb("half", [P, P], BF16)
        rank_bias = sb("rank_bias", [P, GB + 1])
        left_band = sb("left_band", [P, KB + P], BF16)
        spread = sb("spread", [P, KB, P], BF16)
        in_all_row = sb("in_all_row", [P, 1], BF16)
        word_of = sb("word_of", [P, W8], BF16)
        key_base = sb("key_base", [P, KB, W8])
        bit_value = sb("bit_value", [P, 8], I32)
        bit_place = sb("bit_place", [P, 8])
        idx_base = sb("idx_base", [P, NT])
        ones = sb("ones", [P, 1])
        ones_h = sb("ones_h", [P, P], BF16)
        zeros = sb("zeros", [P, 1])
        eps_sb = sb("eps_sb", [P, 1])
        kept_edge = sb("kept_edge", [P, 1])
        ecap_sb = sb("ecap_sb", [P, 1])
        w_sb = sb("w_sb", [P, 2 * KC, OUT])
        bias_sb = sb("bias_sb", [P, OUT])
        bias_h = sb("bias_h", [P, OUT], BF16)
        bias_parts = sb("bias_parts", [P, OUT], BF16)

        adj_sb = sb("adj_sb", [P, 2, N], I32)
        sign_sb = sb("sign_sb", [P, N], BF16)
        mask = sb("mask", [P, KB, P], BF16)
        left = sb("left", [P, P], BF16)
        kept = sb("kept", [P, KB, P], BF16)
        rank = sb("rank", [P, KB, P], BF16)
        pick = sb("pick", [P, 2, L, KB, P], BF16)
        rest = sb("rest", [P, KB, P], BF16)

        xp = sb("xp", [P, 2, KB, 3, C], BF16)
        x_piece = sb("x_piece", [P, 2, C])
        left_over = sb("left_over", [P, 2, C])
        x_sb = sb("x_sb", [P, U, C])

        key = sb("key", [P, KB, W8])
        words = sb("words", [P, 8 * RG])
        words_i = sb("words_i", [P, 8 * RG], I32)
        bit_set = sb("bit_set", [P, 8 * RG, 8], I32)
        word_place = sb("word_place", [P, 8 * RG], I32)
        cand = sb("cand", [P, 8 * RG, 8])
        found = sb("found", [P, U, 8 * RG])
        idx = sb("idx", [P, 2, 8 * RG], I32)
        rows = sb("rows", [P, 2, G + 4, C])
        above = sb("above", [P, U])
        row_max = sb("row_max", [P, C])
        least = sb("least", [P, 1])
        doubt = sb("doubt", [P, U])
        again = sb("again", [1, 2], I32)
        agg = sb("agg", [P, U, C])

        top = sb("top", [P, TOP])
        filled = sb("filled", [P, TOP])
        idx_all = sb("idx_all", [P, TOP], I32)
        floor = sb("floor", [P, 2])
        rows_all = sb("rows_all", [P, S, C])
        place = rows_all[:, 0:N // C, :].rearrange("p k c -> p (k c)")
        score_f = rows_all[:, N // C:2 * N // C, :].rearrange("p k c -> p (k c)")
        score = score_f.bitcast(I32)

        hT = sb("hT", [P, 2 * KC, P])
        z = sb("z", [P, 2, OUT])
        stats = sb("stats", [P, 6])
        mv = sb("mv", [P, 2, 2])
        std = sb("std", [P, 2])
        scale = sb("scale", [P, 2, 2])
        res = sb("res", [P, 2, OUT])

        ps_pick = [pb(f"ps_pick{k}", [P, 4, C]) for k in range(2)]
        ps_work = [pb(f"ps_work{k}", [P, 4 * P]) for k in range(3)]
        ORDER = ("mask0", "mask1", "y", "hT", "row0", "row1", "row2", "row3", "group0", "group1", "group2", "group3")
        bank = {name: ps_work[k % 3] for k, name in enumerate(ORDER)}
        ps_mask = [bank[f"mask{h}"][:].bitcast(BF16).rearrange("p (k r) -> p k r", k=8) for h in range(2)]
        ps_row = [bank[f"row{q}"][:].rearrange("p (k r) -> p k r", k=4) for q in range(NQ)]
        ps_group = [bank[f"group{q}"][:].rearrange("p (k r) -> p k r", k=4) for q in range(NQ)]
        ps_hT = bank["hT"][:].rearrange("p (k r) -> p k r", k=4)
        ps_y = bank["y"][:, 0:OUT]
        ps_misc = pb("ps_misc", [P, 512])
        n_words = KB * W8
        ps_words = ps_misc[:, 0:n_words].rearrange("p (k w) -> p k w", k=KB)
        ps_left = ps_misc[:, n_words:n_words + P]
        ps_count = ps_misc[:, n_words + P:n_words + P + 1]
        ps_again = ps_misc[0:1, n_words + P + 2:n_words + P + 2 + U]

        adj_in = sems("adj_in", 2)
        piece_in = sem("piece_in")
        part_done = sems("part_done", 3)
        over_done = sems("over_done", 2)
        x_in = sems("x_in", U)
        w_in = sem("w_in")
        first_in = sem("first_in")
        rows_in = sems("rows_in", 2)
        out_done = sems("out_done", 2)
        constants = sem("constants")
        halves = sem("halves")
        bias_ready = sem("bias_ready")
        sign_done = sem("sign_done")
        mask_t = sems("mask_t", 2)
        mask_done = sems("mask_done", 2)
        left_sum = sem("left_sum")
        left_done = sem("left_done")
        rank_sum = sems("rank_sum", NQ)
        kept_done = sems("kept_done", NQ)
        code_sum = sems("code_sum", NQ)
        rank_done = sems("rank_done", NQ)
        pick_done = sem("pick_done")
        words_sum = sem("words_sum")
        words_read = sem("words_read")
        chunk_done = sems("chunk_done", NCH)
        chunk_max = sems("chunk_max", NCH)
        zeroed = sem("zeroed")
        idx_ready = sem("idx_ready")
        gather_begun = sem("gather_begun")
        cut_begun = sem("cut_begun")
        redo_begun = sem("redo_begun")
        reduced = sem("reduced")
        doubt_ready = sem("doubt_ready")
        again_sum = sem("again_sum")
        again_ready = sem("again_ready")
        reviewed = sem("reviewed")
        all_adj_in = sem("all_adj_in")
        place_ready = sem("place_ready")
        all_idx_ready = sem("all_idx_ready")
        all_rows_in = sem("all_rows_in")
        all_reduced = sem("all_reduced")
        xp_ready = sem("xp_ready")
        hT_sum = sem("hT_sum")
        hT_done = sem("hT_done")
        y_sum = sem("y_sum")
        residual_done = sem("residual_done")
        std_done = sem("std_done")
        scale_done = sem("scale_done")
        res_done = sem("res_done")
        dve_step = sem("dve_step")

        block = ctx.enter_context(nc.Block())

        def steps(eng, step, last=LAST):
            assert B % 2 == 0
            for s in range(KB):
                step(s // U, s % U, None, 0, s - 2 if s >= 2 else None)
            with eng.Fori(0, B // 2 - 1) as pair:
                for odd in (1, 2):
                    g = 2 * pair + odd
                    for u in range(U):
                        step(TURNS * g, u, g, (odd if u >= 2 else odd - 1) % 2, (u - 2) % KB)
                    with eng.Fori(1, TURNS) as k:
                        for u in range(U):
                            step(TURNS * g + k, u, None, odd % 2, U * k + u - 2)
            for u in range(U):
                step(TURNS * (B - 1), u, B - 1, 1 if u >= 2 else 0, KB - 2 + u if u < 2 else None)
            with eng.Fori(TURNS * (B - 1) + 1, NT // U) as i:
                for u in range(U):
                    step(i, u, None, 1, None)
            for s in range(NT, last):
                step(s // U, s % U, None, 1, None)

        def flat_steps(eng, step, last=LAST):
            for s in range(PEELED * U):
                step(s // U, s % U)
            with eng.Fori(PEELED, NT // U) as i:
                for u in range(U):
                    step(i, u)
            for s in range(NT, last):
                step(s // U, s % U)

        def lagged(i, u, lag):
            if isinstance(i, int):
                t = U * i + u - lag
                return divmod(t, U) if 0 <= t < NT else None
            return i + (u - lag) // U, (u - lag) % U

        def done(eng, sm, t, ago=0):
            if not isinstance(t, int) or t >= ago:
                eng.wait_ge(sm, t - ago + 1)

        def used(i, u):
            return U // 2 * i + u // 2

        def piece(i, u):
            j, half = lagged(i, u, 2)
            return U // 2 * j + half // 2

        @block.sync
        def _(sp):
            sp.dma_start(rows_all[:, 0:KB, :], x[0].rearrange("(k p) c -> p k c", p=P)).then_inc(first_in, 16)
            sp.dma_start(w_sb[:], w.rearrange("(k p) o -> p k o", p=P)).then_inc(w_in, 16)
            sp.dma_start(bias_sb[:], bias.rearrange("(a o) -> a o", a=1).broadcast_to((P, OUT))).then_inc(w_in, 16)

            def load_adj(i, u):
                t, b = U * i + u, u % 2
                done(sp, sign_done, t, 2)
                sp.dma_start(adj_sb[:, b, :], adj_rows[bass.ds(t * P, P), :]).then_inc(adj_in[b], 16)

            def load_piece(j):
                if not isinstance(j, int) or j > 0:
                    sp.wait_ge(over_done[0], j)
                piece = x_rows[bass.ds((KB + 2 * j) * P, 2 * P), :].rearrange("(k p) c -> p k c", p=P)
                sp.dma_start(x_piece[:], piece).then_inc(piece_in, 16)

            def load_x(i, u):
                t = U * i + u
                done(sp, residual_done, t, U)
                sp.dma_start(x_sb[:, u, :], x_rows[bass.ds(t * P, P), :]).then_inc(x_in[u], 16)

            def store(i, u):
                t, b = U * i + u, u % 2
                done(sp, res_done, t)
                sp.dma_start(out_rows[bass.ds(t * P, P), :], res[:, b, :]).then_inc(out_done[b], 16)

            def step(i, u, pieces=True):
                if lagged(i, u, 0):
                    load_adj(i, u)
                    if pieces and u % 2 == 1:
                        load_piece(U // 2 * i + u // 2)
                six, ten = lagged(i, u, 6), lagged(i, u, 10)
                if six:
                    load_x(*six)
                if ten:
                    store(*ten)

            for s in range(PEELED * U):
                step(s // U, s % U)
            with sp.Fori(PEELED, NT // U - TURNS) as i:
                for u in range(U):
                    step(i, u)
            with sp.Fori(NT // U - TURNS, NT // U) as i:
                for u in range(U):
                    step(i, u, False)
            for s in range(NT, NT + 10):
                step(s // U, s % U, False)
            for o in out_done:
                sp.wait_ge(o, 16 * NT // 2)

        @block.gpsimd
        def _(pool):
            made = 0

            def then(ins):
                nonlocal made
                made += 1
                ins.then_inc(constants, 1)
                pool.wait_ge(constants, made)

            def select(ap, pattern, op, fill, base=0, cm=0):
                then(pool.affine_select(out=ap, in_=ap, pattern=pattern, compare_op=op, fill=fill, base=base,
                                        channel_multiplier=cm))

            def identity(m):
                then(pool.memset(m[:], 0.0))
                select(m[:], [[-1, P]], ALU.not_equal, 1.0, cm=1)

            def counting(ap, pattern, base, cm):
                then(pool.iota(ap, pattern=pattern, base=base, channel_multiplier=cm,
                               allow_small_or_imprecise_dtypes=True))

            identity(ident_h)
            for m, one, diag in ((rank_all, 1.0, 1.0 - 4 * CODE), (rank_kept, 0.5, 0.5 + CODE)):
                then(pool.memset(m[:], one))
                select(m[:], [[1, P]], ALU.is_ge, 0.0, cm=-1)
                select(m[:], [[-1, P]], ALU.not_equal, diag, cm=1)
            counting(rank_bias[:, 0:GB], [[P, GB]], 1, 1)
            counting(rank_bias[:, GB:GB + 1], [[0, 1]], 1 + 2 * (L - 1), 1)
            for ap, value in ((half[:], 0.5), (ecap_sb[:], float(ECAP)), (kept_edge[:], S - 4 * CODE - ECAP + 0.5),
                              (left_band[:, 0:KB + 1], 0.0), (left_band[:, KB + 1:KB + P], 1.0), (spread[:], -1.0)):
                then(pool.memset(ap, value))
            select(spread[:], [[-1, KB], [0, P]], ALU.is_equal, 0.0, cm=1)
            assert made == MADE_FIRST, made

            identity(ident)
            then(pool.memset(in_all_row[:], 1.0))
            select(in_all_row[:], [[0, 1]], ALU.is_equal, 0.0, base=-KB, cm=1)
            then(pool.memset(word_of[:], 0.0))
            for k in range(8):
                select(word_of[:], [[-8, W8]], ALU.not_equal, float(2 ** k), base=-k, cm=1)
                then(pool.memset(bit_value[:, k:k + 1], 2 ** k))
            counting(key_base[:], [[-256, NW]], 256 * NW, 0)
            counting(bit_place[:], [[1, 8]], -int(FOUND), 0)
            counting(idx_base[:], [[N, B], [0, KB]], N + int(FOUND), 0)
            for ap, value in ((ones[:], 1.0), (ones_h[:], 1.0), (bias_parts[:], 0.0), (zeros[:], 0.0),
                              (eps_sb[:], EPS)):
                then(pool.memset(ap, value))
            assert made == MADE, made

            def over(j, half, at, n):
                pool.wait_ge(part_done[n], j + 1)
                if n == 0 and (not isinstance(j, int) or j > 0):
                    pool.wait_ge(part_done[2], j)
                pool.sem_inc(cut_begun, 1)
                pool.tensor_tensor(left_over[:], x_piece[:] if n == 0 else left_over[:],
                                   xp[:, half, bass.ds(at, 2), n, :], ALU.subtract).then_inc(over_done[n], 1)

            def gather(i, u):
                t, b = U * i + u, u % 2
                done(pool, idx_ready, t)
                done(pool, zeroed, t)
                pool.sem_inc(gather_begun, 1)
                for k in range(G):
                    pool.indirect_dma_start(
                        out=rows[:, b, k, :], out_offset=None, in_=x_rows,
                        in_offset=bass.IndirectOffsetOnAxis(ap=idx[:, b, k:k + 1], axis=0),
                        bounds_check=B * N - 1, oob_is_err=False,
                    ).then_inc(rows_in[b], 16)

            def redo(i):
                pool.wait_ge(again_ready, i + 1)
                pool.sem_inc(redo_begun, 1)
                flag = pool.value_load(again[0:1, 0:1], min_val=0, max_val=FLAG_MAX)
                with pool.If(flag > 0):
                    for u in range(U):
                        t = U * i + u
                        if u > 0:
                            pool.wait_ge(all_reduced, t)
                            pool.sem_inc(redo_begun, 1)
                        pool.iota(place, pattern=[[-1, N]], base=N, channel_multiplier=0,
                                  allow_small_or_imprecise_dtypes=True).then_inc(place_ready, 1)
                        pool.dma_start(score, adj_rows[bass.ds(t * P, P), :]).then_inc(all_adj_in, 16)
                        pool.wait_ge(all_idx_ready, t + 1)
                        pool.sem_inc(redo_begun, 1)
                        for k in range(S):
                            pool.indirect_dma_start(
                                out=rows_all[:, k, :], out_offset=None, in_=x_rows,
                                in_offset=bass.IndirectOffsetOnAxis(ap=idx_all[:, k:k + 1], axis=0),
                            ).then_inc(all_rows_in, 16)
                with pool.Else():
                    pool.inc_swdge_sem([all_adj_in], [16 * U])
                    pool.inc_swdge_sem([all_rows_in], [16 * S * U])
                pool.wait_ge(reviewed, i + 1)

            def step(i, u, begun, half, at):
                if u == U - 1 and lagged(i, 0, U):
                    redo(i - 1)
                two = lagged(i, u, 2)
                if at is not None:
                    if u % 2 == 0:
                        over(piece(i, u), 1 - half, at, 0)
                    else:
                        over(piece(i, u), 1 - half, at - 1, 1)
                if two:
                    gather(*two)

            steps(pool, step)

        @block.vector
        def _(dve):
            n = 0

            def then(ins):
                nonlocal n
                n += 1
                ins.then_inc(dve_step, 1)
                dve.wait_ge(dve_step, n)

            def free(ins):
                nonlocal n
                n += 1
                ins.then_inc(dve_step, 1)
                return n

            def after(number):
                dve.wait_ge(dve_step, number)

            def fresh():
                nonlocal n
                dve.sem_clear(dve_step)
                n = 0

            first = rows_all[:, 0:KB, :]
            dve.wait_ge(first_in, 16)
            then(dve.tensor_copy(xp[:, 0, :, 0, :], first))
            then(dve.tensor_tensor(first, first, xp[:, 0, :, 0, :], ALU.subtract))
            then(dve.tensor_copy(xp[:, 0, :, 1, :], first))
            then(dve.tensor_tensor(first, first, xp[:, 0, :, 1, :], ALU.subtract))
            then(dve.tensor_copy(xp[:, 0, :, 2, :], first))
            dve.sem_inc(xp_ready, 1)

            dve.wait_ge(constants, MADE)
            dve.wait_ge(w_in, 32)
            for k in range(3):
                then(dve.tensor_copy(bias_h[:], bias_sb[:]))
                then(dve.tensor_copy(bias_parts[32 * k:32 * k + 1, :], bias_sb[32 * k:32 * k + 1, :]))
                if k < 2:
                    then(dve.tensor_tensor(bias_sb[:], bias_sb[:], bias_h[:], ALU.subtract))
            dve.sem_inc(bias_ready, 1)
            fresh()

            def selects(i, u):
                t, b = U * i + u, u % 2
                done(dve, rank_done[NQ - 1], t)
                for q in range(L):
                    last = KB if q == L - 1 else PAIRED
                    free(dve.tensor_scalar(pick[:, b, q, 0:last, :], rank[:, 0:last, :], float(CODE + 1 + q), None,
                                           ALU.is_equal))
                dve.tensor_scalar(rest[:], rank[:], float(CODE + 1 + L), None, ALU.is_ge).then_inc(pick_done, 1)
                after(n)
                fresh()

            def extract(i, u, three, eight):
                t, b = U * i + u, u % 2
                done(dve, words_sum, t)
                based = free(dve.scalar_tensor_tensor(out=key[:], in0=ps_words, scalar=0.0, in1=key_base[:],
                                                      op0=ALU.is_gt, op1=ALU.mult))
                if three:
                    chunk(*three, NCH - 1)
                after(based)
                keyed = free(dve.tensor_tensor(key[:], ps_words, key[:], ALU.add))
                dve.tensor_scalar(above[:, u:u + 1], ps_count, -1.0, float(ECAP - S), ALU.mult,
                                  ALU.add).then_inc(words_read, 1)
                after(keyed)
                for r in range(RG):
                    eight_words = words[:, 8 * r:8 * r + 8]
                    then(dve.max(out=eight_words, in_=key[:]))
                    if r < RG - 1:
                        then(dve.match_replace(out=key[:], in_to_replace=eight_words, in_values=key[:], imm_value=0.0))
                then(dve.tensor_copy(words_i[:], words[:]))
                shape = (P, 8 * RG, 8)
                free(dve.tensor_tensor(bit_set[:], words_i[:].unsqueeze(2).broadcast_to(shape),
                                       bit_value[:].unsqueeze(1).broadcast_to(shape), ALU.bitwise_and))
                placed = free(dve.tensor_scalar(word_place[:], words_i[:], -256, None, ALU.bitwise_and))
                if eight:
                    summed = residual(*eight)
                after(placed)
                raised = free(dve.scalar_tensor_tensor(
                    out=cand[:], in0=word_place[:].unsqueeze(2).broadcast_to(shape), scalar=1.0 / 32.0,
                    in1=bit_place[:].unsqueeze(1).broadcast_to(shape), op0=ALU.mult, op1=ALU.subtract))
                if eight:
                    after(summed)
                    counted = free(dve.bn_stats(out=stats[:], in_=z[:, eight[1] % 2, :]))
                after(raised)
                marked = free(dve.scalar_tensor_tensor(out=cand[:], in0=bit_set[:], scalar=0.0, in1=cand[:],
                                                       op0=ALU.is_gt, op1=ALU.mult))
                if eight:
                    after(counted)
                    moments(*eight)
                after(marked)
                for r in range(RG):
                    eight_found = found[:, u, 8 * r:8 * r + 8]
                    then(dve.max(out=eight_found, in_=cand[:]))
                    if r < RG - 1:
                        then(dve.match_replace(out=cand[:], in_to_replace=eight_found, in_values=cand[:],
                                               imm_value=0.0))
                dve.tensor_scalar(idx[:, b, :], found[:, u, :], -1.0, idx_base[:, bass.ds(t, 1)],
                                  ALU.mult, ALU.add).then_inc(idx_ready, 1)
                fresh()

            def chunk(i, u, c):
                t, b = U * i + u, u % 2
                done(dve, chunk_done[c], t)
                done(dve, chunk_max[c - 1], t)
                dve.tensor_tensor(rows[:, b, G:G + 4, :], rows[:, b, G:G + 4, :], ps_pick[c % 2][:],
                                  ALU.max).then_inc(chunk_max[c], 1)

            def reduce(i, u, eight):
                t, b = U * i + u, u % 2
                dve.wait_ge(rows_in[b], 16 * G * (used(i, u) + 1))
                done(dve, chunk_max[NCH - 1], t)
                dve.tensor_reduce(row_max[:], rows[:, b, :, :].rearrange("p k c -> p c k"), AX_X,
                                  ALU.max).then_inc(reduced, 1)
                done(dve, hT_sum, t, U)
                done(dve, reduced, t)
                final = free(dve.tensor_scalar(agg[:, u, :], row_max[:], 0.0, None, ALU.max, ALU.min,
                                               accum_out=least[:]))
                if eight:
                    inverted = scale_of(*eight)
                done(dve, words_read, t)
                after(final)
                weighed = free(dve.scalar_tensor_tensor(out=least[:], in0=least[:], scalar=0.0, in1=above[:, u:u + 1],
                                                        op0=ALU.is_le, op1=ALU.mult))
                if eight:
                    after(inverted)
                    shift_of(*eight)
                after(weighed)
                dve.tensor_tensor(doubt[:, u:u + 1], least[:], found[:, u, G:G + 1], ALU.max).then_inc(doubt_ready, 1)
                fresh()

            def redo(i, u):
                t = U * i + u
                dve.wait_ge(all_adj_in, 16 * (t + 1))
                dve.wait_ge(place_ready, t + 1)
                then(dve.scalar_tensor_tensor(out=score_f, in0=score, scalar=0.0, in1=place,
                                              op0=ALU.not_equal, op1=ALU.mult))
                for r in range(TOP // 8):
                    eight = top[:, 8 * r:8 * r + 8]
                    then(dve.max(out=eight, in_=score_f))
                    if r < TOP // 8 - 1:
                        then(dve.match_replace(out=score_f, in_to_replace=eight, in_values=score_f, imm_value=0.0))
                then(dve.scalar_tensor_tensor(out=filled[:], in0=top[:], scalar=0.0,
                                              in1=top[:, 0:1].broadcast_to((P, TOP)),
                                              op0=ALU.is_equal, op1=ALU.mult))
                then(dve.tensor_tensor(filled[:], filled[:], top[:], ALU.add))
                then(dve.tensor_scalar(filled[:], filled[:], 1.0, -1.0, ALU.max, ALU.mult))
                then(dve.tensor_scalar(floor[:, 0:1], top[:, S:S + 1], 0.0, -BIG, ALU.is_gt, ALU.mult))
                then(dve.tensor_scalar(floor[:, 1:2], top[:, 0:1], 0.0, BIG, ALU.is_gt, ALU.mult))
                then(dve.tensor_scalar(idx_all[:], filled[:], idx_base[:, bass.ds(t, 1)], -FOUND, ALU.add, ALU.add))
                dve.sem_inc(all_idx_ready, 1)
                dve.wait_ge(all_rows_in, 16 * S * (t + 1))
                then(dve.tensor_reduce(row_max[:], rows_all[:].rearrange("p k c -> p c k"), AX_X, ALU.max))
                dve.sem_inc(all_reduced, 1)
                then(dve.tensor_scalar(agg[:, u, :], row_max[:], floor[:, 0:1], floor[:, 1:2], ALU.max, ALU.min))
                fresh()

            def review(i):
                dve.wait_ge(again_sum, i + 1)
                then(dve.tensor_reduce(again[:, 0:1], ps_again, AX_X, ALU.max))
                dve.sem_inc(again_ready, 1)
                flag = dve.value_load(again[0:1, 0:1], min_val=0, max_val=FLAG_MAX)
                fresh()
                with dve.If(flag > 0):
                    for u in range(U):
                        redo(i, u)
                with dve.Else():
                    dve.sem_inc(place_ready, U)
                    dve.sem_inc(all_idx_ready, U)
                    dve.sem_inc(all_reduced, U)
                dve.sem_inc(reviewed, 1)

            def residual(i, u):
                t, b = U * i + u, u % 2
                done(dve, y_sum, t)
                done(dve, res_done, t, 2)
                return free(dve.scalar_tensor_tensor(out=z[:, b, :], in0=ps_y, scalar=0.0,
                                                     in1=x_sb[:, u, :], op0=ALU.max, op1=ALU.add))

            def moments(i, u):
                dve.bn_aggr(out=mv[:, u % 2, :], in_=stats[:]).then_inc(residual_done, 1)

            def scale_of(i, u):
                b = u % 2
                done(dve, std_done, U * i + u)
                return free(dve.reciprocal(scale[:, b, 0:1], std[:, b:b + 1]))

            def shift_of(i, u):
                b = u % 2
                dve.scalar_tensor_tensor(out=scale[:, b, 1:2], in0=mv[:, b, 0:1], scalar=-1.0, in1=scale[:, b, 0:1],
                                         op0=ALU.mult, op1=ALU.mult).then_inc(scale_done, 1)

            def step(i, u):
                one, two, three, eight = (lagged(i, u, k) for k in (1, 2, 3, 8))
                if three and not two:
                    chunk(*three, NCH - 1)
                if two:
                    extract(*two, three, eight)
                elif eight:
                    after(residual(*eight))
                    then(dve.bn_stats(out=stats[:], in_=z[:, eight[1] % 2, :]))
                    moments(*eight)
                    fresh()
                if three:
                    reduce(*three, eight)
                elif eight:
                    after(scale_of(*eight))
                    shift_of(*eight)
                    fresh()
                if two:
                    chunk(*two, 1)
                if one:
                    selects(*one)
                if two:
                    chunk(*two, 2)
                if u == 2 and lagged(i, 0, U):
                    review(i - 1)

            flat_steps(dve, step)

        @block.scalar
        def _(act):

            def signs(i, u):
                t, b = U * i + u, u % 2
                act.wait_ge(adj_in[b], 16 * (used(i, u) + 1))
                done(act, mask_t[1], t, 1)
                act.activation(sign_sb[:], adj_sb[:, b, :], ACT.Sign).then_inc(sign_done, 1)

            def masks(i, u):
                t = U * i + u
                if isinstance(t, int) and t == 0:
                    act.wait_ge(constants, MADE_FIRST)
                    act.mul(rank_bias[:], rank_bias[:], 0.5).then_inc(halves, 1)
                    act.wait_ge(halves, 1)
                else:
                    act.wait_ge(rank_sum[NQ - 1], t)
                for h in range(2):
                    done(act, mask_t[h], t)
                    act.activation(mask[:, 8 * h:8 * h + 8, :], ps_mask[h], ACT.Square).then_inc(mask_done[h], 1)

            def lefts(i, u):
                t = U * i + u
                done(act, left_sum, t)
                act.activation(left[:], ps_left, ACT.Relu, scale=-1.0,
                               bias=ecap_sb[:, 0:1]).then_inc(left_done, 1)

            def keeps(i, u):
                t = U * i + u
                for q in range(NQ):
                    done(act, rank_sum[q], t)
                    if q == 0:
                        done(act, code_sum[NQ - 1], t, 1)
                    act.activation(kept[:, 4 * q:4 * q + 4, :], ps_row[q], ACT.Sign, scale=-1.0,
                                   bias=kept_edge[:, 0:1]).then_inc(kept_done[q], 1)

            def ranks(i, u):
                t = U * i + u
                for q in range(NQ):
                    done(act, code_sum[q], t)
                    if q == 0:
                        done(act, pick_done, t, 1)
                    if 4 * q >= PAIRED:
                        act.activation(rank[:, 4 * q:4 * q + 4, :], ps_group[q], ACT.Identity,
                                       bias=rank_bias[:, GB:GB + 1]).then_inc(rank_done[q], 1)
                        continue
                    for k in range(GB):
                        last = act.activation(rank[:, 4 * q + k:4 * q + 4:GB, :], ps_group[q][:, k::GB, :],
                                              ACT.Identity, bias=rank_bias[:, k:k + 1])
                    last.then_inc(rank_done[q], 1)

            def first_chunk(i, u):
                t, b = U * i + u, u % 2
                done(act, reduced, t, 2)
                done(act, chunk_done[0], t)
                act.copy(rows[:, b, G:G + 4, :], ps_pick[0][:]).then_inc(chunk_max[0], 1)

            def zero_rows(i, u):
                t, b = U * i + u, u % 2
                if isinstance(t, int) and t == 0:
                    act.wait_ge(constants, MADE)
                done(act, reduced, t, 2)
                act.activation(rows[:, b, 0:G, :].rearrange("p k c -> p (k c)"), zeros[:].broadcast_to((P, G * C)),
                               ACT.Copy).then_inc(zeroed, 1)

            def columns(i, u):
                t = U * i + u
                done(act, hT_sum, t)
                done(act, y_sum, t, 1)
                act.copy(hT[:], ps_hT).then_inc(hT_done, 1)

            def deviation(i, u):
                t, b = U * i + u, u % 2
                done(act, residual_done, t)
                act.activation(std[:, b:b + 1], mv[:, b, 1:2], ACT.Sqrt, bias=eps_sb[:, 0:1]).then_inc(std_done, 1)

            def normalise(i, u):
                t, b = U * i + u, u % 2
                done(act, scale_done, t)
                if not isinstance(i, int) or U * i + u >= 2:
                    act.wait_ge(out_done[b], 16 * used(i, u))
                act.activation(res[:, b, :], z[:, b, :], ACT.Identity, bias=scale[:, b, 1:2],
                               scale=scale[:, b, 0:1]).then_inc(res_done, 1)

            def part(j, half, at, n, begun=None):
                if n == 0:
                    if begun is not None:
                        act.wait_ge(chunk_done[NCH - 1], KB * begun)
                    act.wait_ge(piece_in, 16 * (j + 1))
                else:
                    act.wait_ge(over_done[n - 1], j + 1)
                act.copy(xp[:, half, bass.ds(at, 2), n, :],
                         x_piece[:] if n == 0 else left_over[:]).then_inc(part_done[n], 1)

            def step(i, u, begun, half, at):
                now, one, two, seven, eight, nine = (lagged(i, u, k) for k in (0, 1, 2, 7, 8, 9))
                if at is not None and u % 2 == 1:
                    part(piece(i, u), 1 - half, at - 1, 1)
                if one:
                    masks(*one)
                if now:
                    signs(*now)
                if one:
                    lefts(*one)
                if seven:
                    columns(*seven)
                if at is not None and u % 2 == 0:
                    part(piece(i, u), 1 - half, at, 0, begun if u == 2 else None)
                if two:
                    first_chunk(*two)
                if eight:
                    deviation(*eight)
                if one:
                    keeps(*one)
                if at is not None and u % 2 == 1:
                    part(piece(i, u), 1 - half, at - 1, 2)
                if one:
                    ranks(*one)
                if nine:
                    normalise(*nine)
                if one:
                    zero_rows(*one)

            steps(act, step, LAST + 1)

        @block.tensor
        def _(pe):
            pe.wait_ge(constants, MADE_FIRST)

            def flip(i, u):
                t = U * i + u
                done(pe, sign_done, t)
                for h in range(2):
                    done(pe, rank_done[1 + h], t, 1)
                    for k in range(8):
                        c = 8 * h + k
                        last = pe.transpose(ps_mask[h][:, k, :], sign_sb[:, c * P:(c + 1) * P], ident_h[:])
                    last.then_inc(mask_t[h], 1)

            def count_left(i, u):
                t = U * i + u
                done(pe, words_read, t, 1)
                for c in range(KB):
                    if c % 8 == 0:
                        done(pe, mask_done[c // 8], t)
                    last = pe.matmul(ps_left, left_band[:, KB - c:KB - c + P], mask[:, c, :],
                                     start=(c == 0), stop=(c == KB - 1))
                last.then_inc(left_sum, 1)

            def rank_in_row(i, u, q):
                t = U * i + u
                if q == 0:
                    done(pe, left_done, t)
                elif q == 1:
                    if not isinstance(t, int) or t >= 7:
                        pe.wait_ge(residual_done, t - 6)
                    else:
                        done(pe, rank_done[3], t, 1)
                elif q == 2:
                    if not isinstance(t, int) or t >= 6:
                        pe.wait_ge(hT_done, t - 5)
                elif q == 3:
                    done(pe, kept_done[0], t)
                pe.matmul(ps_row[q], rank_all[:], mask[:, 4 * q:4 * q + 4, :], start=True, stop=False)
                for k in range(4):
                    last = pe.matmul(ps_row[q][:, k, :], spread[:, 4 * q + k, :], left[:], start=False, stop=(k == 3))
                last.then_inc(rank_sum[q], 1)

            def rank_in_group(i, u, q):
                t = U * i + u
                done(pe, kept_done[q], t)
                if q < 3:
                    done(pe, kept_done[q + 1], t)
                else:
                    done(pe, rank_done[0], t)
                more = [(m + k, m + j) for k in range(1, GB) for j in range(k) for m in range(0, 4, GB)]
                if 4 * q >= PAIRED:
                    more = []
                last = pe.matmul(ps_group[q], rank_kept[:], kept[:, 4 * q:4 * q + 4, :], start=True, stop=not more)
                for n, (to, of) in enumerate(more):
                    last = pe.matmul(ps_group[q][:, to, :], half[:], kept[:, 4 * q + of, :],
                                     start=False, stop=(n == len(more) - 1))
                last.then_inc(code_sum[q], 1)

            def word_sums(i, u):
                t = U * i + u
                if isinstance(t, int) and t == 0:
                    pe.wait_ge(constants, MADE)
                done(pe, pick_done, t)
                done(pe, left_done, t)
                for c in range(KB):
                    pe.matmul(ps_words[:, c, :], rest[:, c, :], word_of[:], start=True, stop=True)
                pe.matmul(ps_count, left[:], in_all_row[:], start=True, stop=True).then_inc(words_sum, 1)

            def picks(i, u, half, c, outs=range(4)):
                t, b = U * i + u, u % 2
                if c == 0 and isinstance(t, int) and t == 0:
                    pe.wait_ge(xp_ready, 1)
                if 0 in outs:
                    if c < 2:
                        done(pe, chunk_max[NCH - 2 + c], t, 1)
                    else:
                        done(pe, chunk_max[c - 2], t)
                for o in outs:
                    q, blocks = PICKED[4 * c + o]
                    for k in blocks:
                        for part in range(3):
                            last = pe.matmul(ps_pick[c % 2][:, o, :], pick[:, b, q, k, :], xp[:, half, k, part, :],
                                             start=(k == blocks[0] and part == 0), stop=(k == blocks[-1] and part == 2))
                if 3 in outs:
                    last.then_inc(chunk_done[c], 1)

            def turn_h(i, u):
                t = U * i + u
                pe.wait_ge(x_in[u], 16 * (i + 1))
                if u == 0:
                    pe.wait_ge(reviewed, i + 1)
                if isinstance(t, int) and t + 6 >= NT:
                    pe.wait_ge(rank_done[1], NT)
                    pe.wait_ge(hT_done, t)
                for c in range(KC):
                    pe.transpose(ps_hT[:, c, :], x_sb[:, u, c * P:(c + 1) * P], ident[:])
                for c in range(KC):
                    last = pe.transpose(ps_hT[:, KC + c, :], agg[:, u, c * P:(c + 1) * P], ident[:])
                last.then_inc(hT_sum, 1)

            def output(i, u):
                t = U * i + u
                if isinstance(t, int) and t == 0:
                    pe.wait_ge(w_in, 32)
                    pe.wait_ge(bias_ready, 1)
                done(pe, hT_done, t)
                pe.matmul(ps_y, ones_h[0:65, :], bias_parts[0:65, :], start=True, stop=False)
                for c in range(2 * KC):
                    last = pe.matmul(ps_y, hT[:, c, :], w_sb[:, c, :], start=False, stop=(c == 2 * KC - 1))
                last.then_inc(y_sum, 1)

            def doubts(i):
                pe.wait_ge(doubt_ready, U * (i + 1))
                pe.matmul(ps_again, ones[:], doubt[:], start=True, stop=True).then_inc(again_sum, 1)

            def step(i, u, begun, half, at):
                one, two, seven, eight = (lagged(i, u, k) for k in (1, 2, 7, 8))
                if two:
                    if u == U - 1 and lagged(i, 0, U):
                        pe.wait_ge(again_ready, i)
                    word_sums(*two)
                if one:
                    flip(*one)
                if eight:
                    if two:
                        done(pe, rank_done[3], U * i + u, 2)
                    else:
                        done(pe, residual_done, U * i + u, 9)
                    output(*eight)
                if one:
                    count_left(*one)
                if seven:
                    turn_h(*seven)
                if begun is not None and u == 2:
                    pe.wait_ge(part_done[2], KB // 2 * begun)
                if two:
                    picks(*two, half, 0)
                if one:
                    for q in range(NQ - 1):
                        rank_in_row(*one, q)
                if two:
                    picks(*two, half, 1, range(0, 2))
                if one:
                    rank_in_row(*one, NQ - 1)
                if two:
                    picks(*two, half, 1, range(2, 4))
                if one:
                    for q in range(NQ - 1):
                        rank_in_group(*one, q)
                if two:
                    picks(*two, half, 2, range(0, 2))
                if one:
                    rank_in_group(*one, NQ - 1)
                if two:
                    picks(*two, half, 2, range(2, 4))
                if u == 2 and lagged(i, 0, U):
                    if one:
                        done(pe, left_done, U * i + u, 1)
                    else:
                        pe.wait_ge(words_read, NT)
                    doubts(i - 1)
                if two:
                    picks(*two, half, 3)

            steps(pe, step)


_INS = ["x", "adj", "L0_gnn_W", "L0_gnn_b"]


def kernel(**inputs):
    import numpy as _np
    import concourse.bacc as _bacc
    from concourse import mybir as _mybir
    from concourse.bass_utils import run_bass_kernel_spmd as _run

    nc = _bacc.Bacc("TRN2", target_bir_lowering=False, num_devices=1)
    arrays, args = {}, []
    for name in _INS:
        a = _np.ascontiguousarray(inputs[name])
        arrays[f"in_{name}_dram"] = a
        args.append(nc.dram_tensor(f"in_{name}_dram", a.shape, _mybir.dt.from_np(a.dtype), kind="ExternalInput").ap())
    shape = tuple(inputs["x"].shape)
    args.append(nc.dram_tensor("out_0_dram", shape, _mybir.dt.float32, kind="ExternalOutput").ap())
    build(nc, *args)
    r = _run(nc, [arrays], core_ids=[0])
    return r.results[0]["out_0_dram"]
```
